# Optimizing a Trainium2 kernel written in Bass

```python
import numpy as np
import jax
import jax.numpy as jnp

def _softmax(x, axis=-1):
    return jax.nn.softmax(x, axis=axis)

def _gelu(x):
    return jax.nn.gelu(x, approximate=True)

def _silu(x):
    return jax.nn.silu(x)

def _sigmoid(x):
    return jax.nn.sigmoid(x)

def _layernorm(x, axis=-1, eps=1e-05):
    m = jnp.mean(x, axis=axis, keepdims=True)
    v = jnp.var(x, axis=axis, keepdims=True)
    return (x - m) / jnp.sqrt(v + eps)

def _scatter_add(tgt, idx, src, axis=0):
    return tgt.at[idx].add(src)

def _segment_sum(src, seg, n):
    return jax.ops.segment_sum(src, seg, n)
kernel_name = 'mk_cond_resid_d2_seqx_r4_8e3c13'

def setup_inputs(seed: int=0):
    np.random.seed(seed)
    _w = jnp.asarray

    def _rec_inputs():
        import jax
        import jax.numpy as jnp
        _rk = jax.random.key(seed)
        x = -0.000125 + 0.9999 * jax.random.normal(jax.random.fold_in(_rk, 1), (2, 1024, 256), jnp.float32)
        _lenS = 1024 - jax.random.randint(jax.random.fold_in(_rk, 7), (2,), 0, max(1, 1024 // 4) + 1, jnp.int32)
        _lenS2 = 1024 - jax.random.randint(jax.random.fold_in(_rk, 8), (2,), 0, max(1, 1024 // 4) + 1, jnp.int32)
        itok_B_0_7 = jax.random.randint(jax.random.fold_in(_rk, 11), (2,), 0, 8, jnp.int32)
        return (x, itok_B_0_7)
    x, itok_B_0_7 = _rec_inputs()

    def _L0_cond_setup():
        import jax, jax.numpy as jnp
        import numpy as np
        IN, HID, OUT, PART, E = (256, 1024, 256, 64, 8)
        B, N = (16, 512)
        key = jax.random.key(seed)
        ks = jax.random.split(key, 8)
        s1 = 1.0 / np.sqrt(IN)
        s2 = 1.0 / np.sqrt(HID)
        return {'x': jax.random.normal(ks[0], (B, N, IN), dtype=jnp.float32), 'indices': jax.random.randint(ks[1], (B,), 0, E, dtype=jnp.int64), 'W1': jax.random.uniform(ks[2], (IN, HID), jnp.float32, -s1, s1), 'b1': jax.random.uniform(ks[3], (HID,), jnp.float32, -s1, s1), 'W2': jax.random.uniform(ks[4], (HID, OUT - PART), jnp.float32, -s2, s2), 'b2': jax.random.uniform(ks[5], (OUT - PART,), jnp.float32, -s2, s2), 'We': jax.random.uniform(ks[6], (E, HID, PART), jnp.float32, -s2, s2), 'be': jax.random.uniform(ks[7], (E, PART), jnp.float32, -s2, s2)}
    _L0_cond_all = _L0_cond_setup()
    _L0_cond_in = {k: v for k, v in _L0_cond_all.items() if k in ('W1', 'b1', 'W2', 'b2', 'We', 'be')}
    del _L0_cond_all

    def _L1_cond_setup():
        import jax, jax.numpy as jnp
        import numpy as np
        S, O, H = (8, 256, 256)
        B, N = (32, 128)
        key = jax.random.key(seed)
        k1, k2, k3, k4 = jax.random.split(key, 4)
        x = jax.random.normal(k1, (B, N, H), dtype=jnp.float32)
        subject_id = jax.random.randint(k2, (B,), 0, S)
        wbound = jnp.sqrt(2.0 / 6.0) * jnp.sqrt(3.0 / H)
        weight = jax.random.uniform(k3, (S, O, H), minval=-wbound, maxval=wbound, dtype=jnp.float32)
        bbound = 1.0 / jnp.sqrt(H)
        bias = jax.random.uniform(k4, (S, O), minval=-bbound, maxval=bbound, dtype=jnp.float32)
        return {'x': x, 'subject_id': subject_id, 'weight': weight, 'bias': bias}
    _L1_cond_all = _L1_cond_setup()
    _L1_cond_in = {k: v for k, v in _L1_cond_all.items() if k in ('weight', 'bias')}
    del _L1_cond_all
    return {'x': x, 'itok_B_0_7': itok_B_0_7, 'L0_cond_W1': _L0_cond_in['W1'], 'L0_cond_b1': _L0_cond_in['b1'], 'L0_cond_W2': _L0_cond_in['W2'], 'L0_cond_b2': _L0_cond_in['b2'], 'L0_cond_We': _L0_cond_in['We'], 'L0_cond_be': _L0_cond_in['be'], 'L1_cond_weight': _L1_cond_in['weight'], 'L1_cond_bias': _L1_cond_in['bias']}

def reference(x, itok_B_0_7, L0_cond_W1, L0_cond_b1, L0_cond_W2, L0_cond_b2, L0_cond_We, L0_cond_be, L1_cond_weight, L1_cond_bias):
    import jax
    import jax.numpy as jnp

    def _L0_cond_ref(x, indices, W1, b1, W2, b2, We, be):
        import jax, jax.numpy as jnp
        import numpy as np
        IN, HID, OUT, PART, E = (256, 1024, 256, 64, 8)
        B, N = (16, 512)
        h = jax.nn.gelu(jnp.einsum('bni,ih->bnh', x, W1) + b1, approximate=False)
        shared_x = jnp.einsum('bnh,ho->bno', h, W2) + b2
        We_sel = We[indices]
        be_sel = be[indices]
        expert_x = jnp.einsum('bnh,bhp->bnp', h, We_sel) + be_sel[:, None, :]
        return jnp.concatenate([shared_x, expert_x], axis=-1)

    def _L1_cond_ref(x, subject_id, weight, bias):
        import jax, jax.numpy as jnp
        import numpy as np
        S, O, H = (8, 256, 256)
        B, N = (32, 128)
        W = weight[subject_id]
        b = bias[subject_id]
        y = jnp.einsum('bnh,boh->bno', x, W) + b[:, None, :]
        return y
    x = x + _L0_cond_ref(x, itok_B_0_7, L0_cond_W1, L0_cond_b1, L0_cond_W2, L0_cond_b2, L0_cond_We, L0_cond_be)
    x = x + _L1_cond_ref(x, itok_B_0_7, L1_cond_weight, L1_cond_bias)
    return x

_drawn_inputs = setup_inputs


def setup_inputs(seed=0):
    import zlib

    import numpy as np

    out = dict(_drawn_inputs(seed))
    spreads = {}
    factors = {'L0_cond_b1': 4.805, 'L0_cond_b2': 3.632, 'L0_cond_be': 6.346}
    for name, (base, spread) in spreads.items():
        noise = np.random.default_rng([zlib.crc32(name.encode()), seed]).standard_normal(out[name].shape)
        drawn = base * np.exp(spread * noise) if base else spread * noise
        out[name] = jnp.asarray(drawn.astype(out[name].dtype))
    for name, factor in factors.items():
        out[name] = (out[name] * factor).astype(out[name].dtype)
    return out
```

```python
from contextlib import ExitStack

import concourse.bass as bass
from concourse import mybir

F32 = mybir.dt.float32
F32R = mybir.dt.float32r
I32 = mybir.dt.int32
ACT = mybir.ActivationFunctionType
ALU = mybir.AluOpType

P = 128
TOK = 512
A_BANKS = 4
H_SLOTS = 4
LAG = 2
WARM = 22


def two_layer_kernel(nc, xT, idx, w1, b1, w2, expert_w, expert_b, out):
    NT, _, KI, _ = xT.shape
    _, NJ, _, _ = w1.shape
    B = idx.shape[1]
    E = expert_w.shape[0]
    SH = w2.shape[2]
    D = KI * P
    PART = D - SH
    OC = D // P
    TPB = NT // B
    STEPS = NT * NJ
    W1_PIECES = [(0, 1), (1, 2), (2, 4), (4, 6), (6, 8)]
    V_PIECES = [(0, 2), (2, 4), (4, 8)]

    def piece_of(pieces, j):
        return next(n for n, (lo, hi) in enumerate(pieces) if lo <= j < hi)

    with ExitStack() as ctx:
        def sb(name, shape, dt=F32):
            return ctx.enter_context(nc.sbuf_tensor(name, shape, dt))

        def sem(name):
            return ctx.enter_context(nc.semaphore(name))

        x_raw = sb("x_raw", [P, NT, KI, TOK])
        x_hi = sb("x_hi", [P, NT, KI, TOK], F32R)
        x_lo = sb("x_lo", [P, NT, KI, TOK], F32R)
        w1_raw = sb("w1_raw", [P, NJ, KI, P])
        w1_hi = sb("w1_hi", [P, NJ, KI, P], F32R)
        w1_lo = sb("w1_lo", [P, NJ, KI, P], F32R)
        w2_raw = sb("w2_raw", [P, NJ, SH])
        ex_raw = sb("ex_raw", [P, B, NJ * PART + KI * D])
        v_hi = sb("v_hi", [P, B, NJ, D], F32R)
        v_lo = sb("v_lo", [P, B, NJ, D], F32R)
        l1_hi = sb("l1_hi", [P, B, KI, D], F32R)
        l1_lo = sb("l1_lo", [P, B, KI, D], F32R)
        b1_col = sb("b1_col", [P, NJ])
        eb_col = sb("eb_col", [P, B, 2 * KI])
        idx_sb = sb("idx_sb", [1, B], I32)
        h_full = sb("h_full", [P, H_SLOTS, TOK])
        h_hi = sb("h_hi", [P, H_SLOTS, TOK], F32R)
        h_lo = sb("h_lo", [P, H_SLOTS, TOK], F32R)
        x1_full = sb("x1_full", [P, 2, OC, TOK])
        x1_hi = sb("x1_hi", [P, 2, OC, TOK], F32R)
        x1_lo = sb("x1_lo", [P, 2, OC, TOK], F32R)
        o_sb = sb("o_sb", [P, 2, OC, TOK])
        warm = sb("warm", [P, TOK], mybir.dt.bfloat16)
        warm_act = sb("warm_act", [P, 1])

        a_ps = [ctx.enter_context(nc.psum_tensor(f"a_ps{n}", [P, TOK], F32)) for n in range(A_BANKS)]
        y_ps = [ctx.enter_context(nc.psum_tensor(f"y_ps{n}", [P, TOK], F32)) for n in range(OC)]
        z_ps = [ctx.enter_context(nc.psum_tensor(f"z_ps{n}", [P, TOK], F32)) for n in range(OC)]

        idx_in = sem("idx_in")
        b1_in = sem("b1_in")
        w1_in = [sem(f"w1_in{n}") for n in range(len(W1_PIECES))]
        x_in = [[sem(f"x_in{t}_{k}") for k in range(KI)] for t in range(NT)]
        w2_in = [sem(f"w2_in{n}") for n in range(len(V_PIECES))]
        ex_in = [sem(f"ex_in{b}") for b in range(B)]
        eb_in = [sem(f"eb_in{b}") for b in range(B)]
        warm_set = sem("warm_set")
        x_hi_ready = sem("x_hi_ready")
        x_lo_ready = sem("x_lo_ready")
        w1_hi_ready = sem("w1_hi_ready")
        w1_lo_ready = sem("w1_lo_ready")
        v_hi_ready = sem("v_hi_ready")
        v_lo_ready = sem("v_lo_ready")
        l1_hi_ready = sem("l1_hi_ready")
        l1_lo_ready = sem("l1_lo_ready")
        a_done = sem("a_done")
        gelu_done = sem("gelu_done")
        h_ready = sem("h_ready")
        b_done = sem("b_done")
        y_done = sem("y_done")
        x1_ready = sem("x1_ready")
        x1_hi_ready = sem("x1_hi_ready")
        x1_lo_ready = sem("x1_lo_ready")
        z_done = sem("z_done")
        o_ready = sem("o_ready")
        stored = [sem(f"stored{n}") for n in range(2)]

        block = ctx.enter_context(nc.Block())

        @block.sync
        def _(sp):
            def load_w1(n):
                lo, hi = W1_PIECES[n]
                sp.dma_start(w1_raw[:, lo:hi], w1[:, lo:hi]).then_inc(w1_in[n], 16)

            def load_w2(n):
                lo, hi = V_PIECES[n]
                sp.dma_start(w2_raw[:, lo:hi], w2[:, lo:hi]).then_inc(w2_in[n], 16)

            def load_x(t, k):
                sp.dma_start(x_raw[:, t, k], xT[t, :, k]).then_inc(x_in[t][k], 16)

            load_w1(0)
            load_x(0, 0)
            load_x(0, 1)
            load_w1(1)
            sp.dma_start(idx_sb[:], idx).then_inc(idx_in, 16)
            sp.dma_start(b1_col[:], b1).then_inc(b1_in, 16)
            load_w1(2)
            load_w2(0)
            sp.wait_ge(idx_in, 16)
            expert = [sp.value_load(idx_sb[0:1, b:b + 1], min_val=0, max_val=E - 1) for b in range(B)]

            def load_expert(b):
                sp.dma_start(ex_raw[:, b], expert_w[bass.ds(expert[b], 1)].rearrange("e p n -> p (e n)"))\
                    .then_inc(ex_in[b], 16)
                sp.dma_start(eb_col[:, b], expert_b[bass.ds(expert[b], 1)].rearrange("e p n -> p (e n)"))\
                    .then_inc(eb_in[b], 16)

            load_expert(0)
            load_w1(3)
            load_w2(1)
            load_w1(4)
            load_w2(2)
            for t in range(1, NT):
                for k in range(KI):
                    load_x(t, k)
                if t < B:
                    load_expert(t)
            for t in range(NT):
                for c in range(OC):
                    sp.wait_ge(o_ready, OC * t + c + 1)
                    sp.dma_start(out[t, :, c], o_sb[:, t % 2, c]).then_inc(stored[t % 2], 16)
            for n in range(2):
                sp.wait_ge(stored[n], 16 * OC * (NT // 2))

        def w2_of(n):
            lo, hi = V_PIECES[n]
            return w2_raw[:, lo:hi]

        def we_of(b, n):
            lo, hi = V_PIECES[n]
            return ex_raw[:, b, 0:NJ * PART].rearrange("p (j c) -> p j c", j=NJ)[:, lo:hi]

        def l1_of(b):
            return ex_raw[:, b, NJ * PART:].rearrange("p (k c) -> p k c", k=KI)

        @block.scalar
        def _(act):
            def split_x_hi(t):
                for k in range(KI):
                    act.wait_ge(x_in[t][k], 16)
                    nc.scalar.activation(x_hi[:, t, k], x_raw[:, t, k], ACT.Copy).then_inc(x_hi_ready, 1)

            def split_w1_hi(n):
                lo, hi = W1_PIECES[n]
                act.wait_ge(w1_in[n], 16)
                nc.scalar.activation(w1_hi[:, lo:hi], w1_raw[:, lo:hi], ACT.Copy).then_inc(w1_hi_ready, 1)

            def split_v_hi(b, n):
                lo, hi = V_PIECES[n]
                act.wait_ge(w2_in[n], 16)
                nc.scalar.activation(v_hi[:, b, lo:hi, 0:SH], w2_of(n), ACT.Copy).then_inc(v_hi_ready, 1)
                act.wait_ge(ex_in[b], 16)
                nc.scalar.activation(v_hi[:, b, lo:hi, SH:D], we_of(b, n), ACT.Copy).then_inc(v_hi_ready, 1)

            def split_l1_hi(b):
                act.wait_ge(ex_in[b], 16)
                nc.scalar.activation(l1_hi[:, b], l1_of(b), ACT.Copy).then_inc(l1_hi_ready, 1)

            def gelu(s):
                act.wait_ge(a_done, s + 1)
                if s >= H_SLOTS:
                    act.wait_ge(b_done, s - H_SLOTS + 1)
                j = s % NJ
                nc.scalar.activation(h_hi[:, s % H_SLOTS], a_ps[s % A_BANKS][:], ACT.Gelu, bias=b1_col[:, j:j + 1])
                nc.scalar.activation(h_full[:, s % H_SLOTS], a_ps[s % A_BANKS][:], ACT.Gelu,
                                     bias=b1_col[:, j:j + 1]).then_inc(gelu_done, 1)

            def split_x1_hi(t):
                for c in range(OC):
                    act.wait_ge(x1_ready, OC * t + c + 1)
                    if t >= 2:
                        act.wait_ge(z_done, OC * (t - 1))
                    nc.scalar.activation(x1_hi[:, t % 2, c], x1_full[:, t % 2, c], ACT.Copy).then_inc(x1_hi_ready, 1)

            act.wait_ge(warm_set, 2)
            nc.scalar.activation(warm_act[:], warm_act[:], ACT.Gelu)
            split_w1_hi(0)
            split_x_hi(0)
            for n in range(1, 3):
                split_w1_hi(n)
            act.wait_ge(b1_in, 16)
            split_v_hi(0, 0)
            gelu(0)
            split_w1_hi(3)
            split_v_hi(0, 1)
            gelu(1)
            split_w1_hi(4)
            gelu(2)
            split_v_hi(0, 2)
            extra = {4: lambda: split_l1_hi(0), 5: lambda: split_x_hi(1)}
            for n in range(len(V_PIECES)):
                extra[NJ * TPB - 5 + n] = lambda n=n: split_v_hi(1, n)
            extra[NJ * TPB - 2] = lambda: split_l1_hi(1)
            for t in range(2, NT):
                extra[NJ * (t - 1) + 2] = lambda t=t: split_x_hi(t)
            for s in range(3, STEPS):
                gelu(s)
                if s in extra:
                    extra[s]()
                if s % NJ == LAG and s > NJ:
                    split_x1_hi(s // NJ - 1)
            split_x1_hi(NT - 1)

        @block.vector
        def _(dve):
            def split_x_lo(t):
                for k in range(KI):
                    dve.wait_ge(x_hi_ready, KI * t + k + 1)
                    nc.vector.tensor_tensor(x_lo[:, t, k], x_raw[:, t, k], x_hi[:, t, k].bitcast(F32),
                                            ALU.subtract).then_inc(x_lo_ready, 1)

            def split_w1_lo(n):
                lo, hi = W1_PIECES[n]
                dve.wait_ge(w1_hi_ready, n + 1)
                nc.vector.tensor_tensor(w1_lo[:, lo:hi], w1_raw[:, lo:hi], w1_hi[:, lo:hi].bitcast(F32),
                                        ALU.subtract).then_inc(w1_lo_ready, 1)

            def split_v_lo(b, n):
                lo, hi = V_PIECES[n]
                dve.wait_ge(v_hi_ready, 2 * (b * len(V_PIECES) + n) + 1)
                nc.vector.tensor_tensor(v_lo[:, b, lo:hi, 0:SH], w2_of(n),
                                        v_hi[:, b, lo:hi, 0:SH].bitcast(F32), ALU.subtract).then_inc(v_lo_ready, 1)
                dve.wait_ge(v_hi_ready, 2 * (b * len(V_PIECES) + n) + 2)
                nc.vector.tensor_tensor(v_lo[:, b, lo:hi, SH:D], we_of(b, n),
                                        v_hi[:, b, lo:hi, SH:D].bitcast(F32), ALU.subtract).then_inc(v_lo_ready, 1)

            def split_l1_lo(b):
                dve.wait_ge(l1_hi_ready, b + 1)
                nc.vector.tensor_tensor(l1_lo[:, b], l1_of(b), l1_hi[:, b].bitcast(F32),
                                        ALU.subtract).then_inc(l1_lo_ready, 1)

            def split_h(s):
                dve.wait_ge(gelu_done, s + 1)
                n = s % H_SLOTS
                nc.vector.tensor_tensor(h_lo[:, n], h_full[:, n], h_hi[:, n].bitcast(F32),
                                        ALU.subtract).then_inc(h_ready, 1)

            def residual_x1(t):
                b = t // TPB
                for c in range(OC):
                    dve.wait_ge(y_done, OC * t + c + 1)
                    if c == 0 and t % TPB == 0:
                        dve.wait_ge(eb_in[b], 16)
                    nc.vector.scalar_tensor_tensor(x1_full[:, t % 2, c], y_ps[c][:], eb_col[:, b, c:c + 1],
                                                   x_raw[:, t, c], ALU.add, ALU.add).then_inc(x1_ready, 1)
                for c in range(OC):
                    dve.wait_ge(x1_hi_ready, OC * t + c + 1)
                    nc.vector.tensor_tensor(x1_lo[:, t % 2, c], x1_full[:, t % 2, c],
                                            x1_hi[:, t % 2, c].bitcast(F32), ALU.subtract).then_inc(x1_lo_ready, 1)

            def residual_out(t):
                b = t // TPB
                for c in range(OC):
                    dve.wait_ge(z_done, OC * t + c + 1)
                    if t >= 2:
                        dve.wait_ge(stored[t % 2], 16 * OC * (t // 2))
                    nc.vector.scalar_tensor_tensor(o_sb[:, t % 2, c], z_ps[c][:], eb_col[:, b, OC + c:OC + c + 1],
                                                   x1_full[:, t % 2, c], ALU.add, ALU.add).then_inc(o_ready, 1)

            nc.vector.memset(warm[:], 0.0).then_inc(warm_set, 1)
            nc.vector.memset(warm_act[:], 0.0).then_inc(warm_set, 1)
            split_w1_lo(0)
            split_x_lo(0)
            split_w1_lo(1)
            split_w1_lo(2)
            split_v_lo(0, 0)
            split_h(0)
            split_w1_lo(3)
            split_v_lo(0, 1)
            split_h(1)
            split_w1_lo(4)
            split_h(2)
            split_v_lo(0, 2)
            extra = {4: lambda: split_l1_lo(0), 5: lambda: split_x_lo(1)}
            for n in range(len(V_PIECES)):
                extra[NJ * TPB - 5 + n] = lambda n=n: split_v_lo(1, n)
            extra[NJ * TPB - 2] = lambda: split_l1_lo(1)
            for t in range(2, NT):
                extra[NJ * (t - 1) + 2] = lambda t=t: split_x_lo(t)
            for s in range(3, STEPS):
                split_h(s)
                if s in extra:
                    extra[s]()
                if s % NJ == LAG and s > NJ:
                    residual_x1(s // NJ - 1)
                if s % NJ == LAG + 2 and s > NJ:
                    residual_out(s // NJ - 1)
            residual_x1(NT - 1)
            residual_out(NT - 1)

        @block.tensor
        def _(pe):
            def product_a(s):
                t, j = divmod(s, NJ)
                if s >= A_BANKS:
                    pe.wait_ge(gelu_done, s - A_BANKS + 1)
                n = piece_of(W1_PIECES, j)
                for k in range(KI):
                    if t == 0:
                        pe.wait_ge(w1_hi_ready, n + 1)
                    if j == 0:
                        pe.wait_ge(x_hi_ready, KI * t + k + 1)
                    nc.tensor.matmul(a_ps[s % A_BANKS][:], w1_hi[:, j, k], x_hi[:, t, k], start=(k == 0), stop=False)
                    if t == 0:
                        pe.wait_ge(w1_lo_ready, n + 1)
                    nc.tensor.matmul(a_ps[s % A_BANKS][:], w1_lo[:, j, k], x_hi[:, t, k], start=False, stop=False)
                    if j == 0:
                        pe.wait_ge(x_lo_ready, KI * t + k + 1)
                    last = nc.tensor.matmul(a_ps[s % A_BANKS][:], w1_hi[:, j, k], x_lo[:, t, k],
                                            start=False, stop=(k == KI - 1))
                last.then_inc(a_done, 1)

            def product_b(s):
                t, j = divmod(s, NJ)
                b = t // TPB
                pe.wait_ge(h_ready, s + 1)
                if t % TPB == 0:
                    pe.wait_ge(v_lo_ready, 2 * (b * len(V_PIECES) + piece_of(V_PIECES, j)) + 2)
                n = s % H_SLOTS
                for c in range(OC):
                    if j == 0 and t >= 1:
                        pe.wait_ge(x1_ready, OC * (t - 1) + c + 1)
                    cols = slice(c * P, (c + 1) * P)
                    nc.tensor.matmul(y_ps[c][:], v_lo[:, b, j, cols], h_hi[:, n], start=(j == 0), stop=False)
                    nc.tensor.matmul(y_ps[c][:], v_hi[:, b, j, cols], h_hi[:, n], start=False, stop=False)
                    last = nc.tensor.matmul(y_ps[c][:], v_hi[:, b, j, cols], h_lo[:, n], start=False, stop=(j == NJ - 1))
                    if j == NJ - 1:
                        last.then_inc(y_done, 1)
                    elif c == OC - 1:
                        last.then_inc(b_done, 1)
                if j == NJ - 1:
                    nc.tensor.nop().then_inc(b_done, 1)

            def product_c(t):
                b = t // TPB
                if t % TPB == 0:
                    pe.wait_ge(l1_lo_ready, b + 1)
                for k in range(KI):
                    pe.wait_ge(x1_lo_ready, OC * t + k + 1)
                    for c in range(OC):
                        if k == 0 and t >= 1:
                            pe.wait_ge(o_ready, OC * (t - 1) + c + 1)
                        cols = slice(c * P, (c + 1) * P)
                        nc.tensor.matmul(z_ps[c][:], l1_lo[:, b, k, cols], x1_hi[:, t % 2, k], start=(k == 0), stop=False)
                        nc.tensor.matmul(z_ps[c][:], l1_hi[:, b, k, cols], x1_hi[:, t % 2, k], start=False, stop=False)
                        last = nc.tensor.matmul(z_ps[c][:], l1_hi[:, b, k, cols], x1_lo[:, t % 2, k],
                                                start=False, stop=(k == KI - 1))
                        if k == KI - 1:
                            last.then_inc(z_done, 1)

            pe.wait_ge(warm_set, 1)
            for _ in range(WARM):
                nc.tensor.matmul(z_ps[0][:], warm[:, 0:P], warm[:], start=True, stop=True)
            for s in range(STEPS + LAG):
                if s < STEPS:
                    product_a(s)
                if s % NJ == LAG and s > NJ:
                    product_c(s // NJ - 1)
                if s >= LAG:
                    product_b(s - LAG)
            product_c(NT - 1)


def kernel(x, itok_B_0_7, L0_cond_W1, L0_cond_b1, L0_cond_W2, L0_cond_b2, L0_cond_We, L0_cond_be,
           L1_cond_weight, L1_cond_bias):
    import numpy as np
    import concourse.bacc as bacc
    from concourse.bass_utils import run_bass_kernel_spmd

    x, idx, W1, b1, W2, b2, We, be, L1, l1b = (np.asarray(a) for a in (
        x, itok_B_0_7, L0_cond_W1, L0_cond_b1, L0_cond_W2, L0_cond_b2, L0_cond_We, L0_cond_be,
        L1_cond_weight, L1_cond_bias))
    B, N, D = x.shape
    HID = W1.shape[1]
    E, _, PART = We.shape
    KI, NJ, NT = D // P, HID // P, B * N // TOK

    xT = x.reshape(NT, TOK, KI, P).transpose(0, 3, 2, 1)
    w1 = W1.reshape(KI, P, NJ, P).transpose(1, 2, 0, 3)
    b1c = b1.reshape(NJ, P).T
    w2 = W2.reshape(NJ, P, D - PART).transpose(1, 0, 2)
    we = We.reshape(E, NJ, P, PART).transpose(0, 2, 1, 3).reshape(E, P, NJ * PART)
    l1 = L1.transpose(0, 2, 1).reshape(E, KI, P, D).transpose(0, 2, 1, 3).reshape(E, P, KI * D)
    expert_w = np.concatenate([we, l1], axis=2)
    yb = np.concatenate([np.broadcast_to(b2, (E, D - PART)), be], axis=1).reshape(E, KI, P).transpose(0, 2, 1)
    zb = l1b.reshape(E, KI, P).transpose(0, 2, 1)
    expert_b = np.concatenate([yb, zb], axis=2)

    nc = bacc.Bacc("TRN2", target_bir_lowering=False, num_devices=1)
    arrays, aps = {}, []
    for name, a in [("xT", xT), ("idx", idx.reshape(1, B)), ("w1", w1), ("b1", b1c), ("w2", w2),
                    ("expert_w", expert_w), ("expert_b", expert_b)]:
        a = np.ascontiguousarray(a)
        arrays[name] = a
        aps.append(nc.dram_tensor(name, a.shape, mybir.dt.from_np(a.dtype), kind="ExternalInput").ap())
    out = nc.dram_tensor("out", (NT, P, KI, TOK), F32, kind="ExternalOutput").ap()
    two_layer_kernel(nc, *aps, out)
    r = run_bass_kernel_spmd(nc, [arrays], core_ids=[0])
    got = np.asarray(r.results[0]["out"])
    return np.ascontiguousarray(got.transpose(0, 3, 2, 1)).reshape(B, N, D)
```

```python
from contextlib import ExitStack

import concourse.bass as bass
from concourse import mybir

F32 = mybir.dt.float32
F32R = mybir.dt.float32r
I32 = mybir.dt.int32
ACT = mybir.ActivationFunctionType
ALU = mybir.AluOpType

P = 128
TOK = 512
A_BANKS = 4
H_SLOTS = 5
LAG = 3
WARM = 28


def two_layer_kernel(nc, xT, idx, w1, b1, w2, expert_w, expert_b, out):
    NT, _, KI, _ = xT.shape
    _, NJ, _, _ = w1.shape
    B = idx.shape[1]
    E = expert_w.shape[0]
    SH = w2.shape[2]
    D = KI * P
    PART = D - SH
    OC = D // P
    TPB = NT // B
    STEPS = NT * NJ
    W1_PIECES = [(0, 1), (1, 2), (2, 4), (4, 6), (6, 8)]
    V_PIECES = [(0, 2), (2, 4), (4, 8)]

    def piece_of(pieces, j):
        return next(n for n, (lo, hi) in enumerate(pieces) if lo <= j < hi)

    with ExitStack() as ctx:
        def sb(name, shape, dt=F32):
            return ctx.enter_context(nc.sbuf_tensor(name, shape, dt))

        def sem(name):
            return ctx.enter_context(nc.semaphore(name))

        x_raw = sb("x_raw", [P, NT, KI, TOK])
        x_hi = sb("x_hi", [P, NT, KI, TOK], F32R)
        x_lo = sb("x_lo", [P, NT, KI, TOK], F32R)
        w1_raw = sb("w1_raw", [P, NJ, KI, P])
        w1_hi = sb("w1_hi", [P, NJ, KI, P], F32R)
        w1_lo = sb("w1_lo", [P, NJ, KI, P], F32R)
        w2_raw = sb("w2_raw", [P, NJ, SH])
        ex_raw = sb("ex_raw", [P, B, NJ * PART + KI * D])
        v_hi = sb("v_hi", [P, B, NJ, D], F32R)
        v_lo = sb("v_lo", [P, B, NJ, D], F32R)
        l1_hi = sb("l1_hi", [P, B, KI, D], F32R)
        l1_lo = sb("l1_lo", [P, B, KI, D], F32R)
        b1_col = sb("b1_col", [P, NJ])
        eb_col = sb("eb_col", [P, B, 2 * KI])
        idx_sb = sb("idx_sb", [1, B], I32)
        h_full = sb("h_full", [P, H_SLOTS, TOK])
        h_hi = sb("h_hi", [P, H_SLOTS, TOK], F32R)
        h_lo = sb("h_lo", [P, H_SLOTS, TOK], F32R)
        x1_full = sb("x1_full", [P, 2, OC, TOK])
        x1_hi = sb("x1_hi", [P, 2, OC, TOK], F32R)
        x1_lo = sb("x1_lo", [P, 2, OC, TOK], F32R)
        o_sb = sb("o_sb", [P, 2, OC, TOK])
        warm = sb("warm", [P, P], mybir.dt.bfloat16)
        warm_act = sb("warm_act", [P, 1])

        a_ps = [ctx.enter_context(nc.psum_tensor(f"a_ps{n}", [P, TOK], F32)) for n in range(A_BANKS)]
        y_ps = [ctx.enter_context(nc.psum_tensor(f"y_ps{n}", [P, TOK], F32)) for n in range(OC)]
        z_ps = [ctx.enter_context(nc.psum_tensor(f"z_ps{n}", [P, TOK], F32)) for n in range(OC)]

        def out_parts(t):
            if t < NT - 1:
                return [(c, slice(0, TOK), z_ps[c]) for c in range(OC)]
            whole = [(c, slice(0, TOK), z_ps[c]) for c in range(OC - 1)]
            return whole + [(OC - 1, slice(0, TOK // 2), z_ps[OC - 1]), (OC - 1, slice(TOK // 2, TOK), a_ps[0])]

        idx_in = sem("idx_in")
        b1_in = sem("b1_in")
        w1_in = [sem(f"w1_in{n}") for n in range(len(W1_PIECES))]
        x_in = [[sem(f"x_in{t}_{k}") for k in range(KI)] for t in range(NT)]
        w2_in = [sem(f"w2_in{n}") for n in range(len(V_PIECES))]
        ex_in = [sem(f"ex_in{b}") for b in range(B)]
        eb_in = [sem(f"eb_in{b}") for b in range(B)]
        warm_set = sem("warm_set")
        x_hi_ready = [[sem(f"x_hi_ready{t}_{k}") for k in range(KI)] for t in range(NT)]
        x_lo_ready = sem("x_lo_ready")
        w1_hi_ready = sem("w1_hi_ready")
        w1_first_ready = sem("w1_first_ready")
        w1_lo_ready = sem("w1_lo_ready")
        v_hi_ready = sem("v_hi_ready")
        v_lo_ready = sem("v_lo_ready")
        l1_hi_ready = sem("l1_hi_ready")
        l1_lo_ready = sem("l1_lo_ready")
        a_done = sem("a_done")
        gelu_done = sem("gelu_done")
        h_ready = sem("h_ready")
        b_done = sem("b_done")
        y_done = sem("y_done")
        x1_ready = sem("x1_ready")
        x1_hi_ready = sem("x1_hi_ready")
        x1_last_hi = sem("x1_last_hi")
        x1_lo_ready = sem("x1_lo_ready")
        z_done = sem("z_done")
        o_ready = sem("o_ready")
        stored = [sem(f"stored{n}") for n in range(2)]

        block = ctx.enter_context(nc.Block())

        @block.sync
        def _(sp):
            def load_w1(n):
                lo, hi = W1_PIECES[n]
                sp.dma_start(w1_raw[:, lo:hi], w1[:, lo:hi]).then_inc(w1_in[n], 16)

            def load_w2(n):
                lo, hi = V_PIECES[n]
                sp.dma_start(w2_raw[:, lo:hi], w2[:, lo:hi]).then_inc(w2_in[n], 16)

            def load_x(t, k):
                sp.dma_start(x_raw[:, t, k], xT[t, :, k]).then_inc(x_in[t][k], 16)

            load_x(0, 0)
            load_w1(0)
            load_x(0, 1)
            load_w1(1)
            load_w1(2)
            load_w2(0)
            sp.wait_ge(idx_in, 16)
            expert = [sp.value_load(idx_sb[0:1, b:b + 1], min_val=0, max_val=E - 1) for b in range(B)]

            def load_expert(b):
                sp.dma_start(ex_raw[:, b], expert_w[bass.ds(expert[b], 1)].rearrange("e p n -> p (e n)"))\
                    .then_inc(ex_in[b], 16)
                sp.dma_start(eb_col[:, b], expert_b[bass.ds(expert[b], 1)].rearrange("e p n -> p (e n)"))\
                    .then_inc(eb_in[b], 16)

            load_expert(0)
            load_w1(3)
            load_w2(1)
            load_w1(4)
            load_w2(2)
            for t in range(1, NT):
                for k in range(KI):
                    load_x(t, k)
                if t < B:
                    load_expert(t)
            for t in range(NT):
                for n, (c, cols, _) in enumerate(out_parts(t)):
                    sp.wait_ge(o_ready, OC * t + n + 1)
                    sp.dma_start(out[t, :, c, cols], o_sb[:, t % 2, c, cols]).then_inc(stored[t % 2], 16)
            for n in range(2):
                sp.wait_ge(stored[n], 16 * sum(len(out_parts(t)) for t in range(n, NT, 2)))

        def w2_of(n):
            lo, hi = V_PIECES[n]
            return w2_raw[:, lo:hi]

        def we_of(b, n):
            lo, hi = V_PIECES[n]
            return ex_raw[:, b, 0:NJ * PART].rearrange("p (j c) -> p j c", j=NJ)[:, lo:hi]

        def l1_of(b):
            return ex_raw[:, b, NJ * PART:].rearrange("p (k c) -> p k c", k=KI)

        @block.gpsimd
        def _(pool):
            pool.dma_start(idx_sb[:], idx).then_inc(idx_in, 16)
            pool.dma_start(b1_col[:], b1).then_inc(b1_in, 16)

        @block.scalar
        def _(act):
            def split_x_hi(t, k):
                act.wait_ge(x_in[t][k], 16)
                nc.scalar.activation(x_hi[:, t, k], x_raw[:, t, k], ACT.Copy).then_inc(x_hi_ready[t][k], 1)

            def split_w1_hi(n):
                lo, hi = W1_PIECES[n]
                act.wait_ge(w1_in[n], 16)
                nc.scalar.activation(w1_hi[:, lo:hi], w1_raw[:, lo:hi], ACT.Copy).then_inc(w1_hi_ready, 1)

            def split_v_hi(b, n):
                lo, hi = V_PIECES[n]
                act.wait_ge(w2_in[n], 16)
                nc.scalar.activation(v_hi[:, b, lo:hi, 0:SH], w2_of(n), ACT.Copy).then_inc(v_hi_ready, 1)
                act.wait_ge(ex_in[b], 16)
                nc.scalar.activation(v_hi[:, b, lo:hi, SH:D], we_of(b, n), ACT.Copy).then_inc(v_hi_ready, 1)

            def split_l1_hi(b):
                act.wait_ge(ex_in[b], 16)
                nc.scalar.activation(l1_hi[:, b], l1_of(b), ACT.Copy).then_inc(l1_hi_ready, 1)

            def gelu(s):
                act.wait_ge(a_done, s + 1)
                if s >= H_SLOTS:
                    act.wait_ge(b_done, s - H_SLOTS + 1)
                j = s % NJ
                nc.scalar.activation(h_hi[:, s % H_SLOTS], a_ps[s % A_BANKS][:], ACT.Gelu, bias=b1_col[:, j:j + 1])
                nc.scalar.activation(h_full[:, s % H_SLOTS], a_ps[s % A_BANKS][:], ACT.Gelu,
                                     bias=b1_col[:, j:j + 1]).then_inc(gelu_done, 1)

            def split_x1_hi(t):
                for c in range(OC):
                    act.wait_ge(x1_ready, OC * t + c + 1)
                    if t >= 2:
                        act.wait_ge(z_done, OC * (t - 1))
                    nc.scalar.activation(x1_hi[:, t % 2, c], x1_full[:, t % 2, c], ACT.Copy).then_inc(x1_hi_ready, 1)

            act.wait_ge(warm_set, 2)
            nc.scalar.activation(warm_act[:], warm_act[:], ACT.Gelu)
            split_x_hi(0, 1)
            split_w1_hi(1)
            split_w1_hi(2)
            split_v_hi(0, 0)
            act.wait_ge(b1_in, 16)
            extra = {0: [(split_w1_hi, 3)], 1: [(split_w1_hi, 4), (split_v_hi, 0, 1)], 2: [(split_v_hi, 0, 2)],
                     4: [(split_l1_hi, 0)]}
            for t in range(1, NT):
                extra[NJ * (t - 1) + 5] = [(split_x_hi, t, k) for k in range(KI)]
            for n in range(len(V_PIECES)):
                extra[NJ * (TPB - 1) + n] = [(split_v_hi, 1, n)]
            extra[NJ * (TPB - 1) + 4] = [(split_l1_hi, 1)]
            for s in range(STEPS):
                if s % NJ == LAG and s > NJ:
                    split_x1_hi(s // NJ - 1)
                gelu(s)
                for split, *args in extra.get(s, ()):
                    split(*args)

        @block.vector
        def _(dve):
            def split_x_lo(t, k):
                dve.wait_ge(x_hi_ready[t][k], 1)
                nc.vector.tensor_tensor(x_lo[:, t, k], x_raw[:, t, k], x_hi[:, t, k].bitcast(F32),
                                        ALU.subtract).then_inc(x_lo_ready, 1)

            def split_w1_lo(n):
                lo, hi = W1_PIECES[n]
                if n == 0:
                    dve.wait_ge(w1_first_ready, 1)
                else:
                    dve.wait_ge(w1_hi_ready, n)
                nc.vector.tensor_tensor(w1_lo[:, lo:hi], w1_raw[:, lo:hi], w1_hi[:, lo:hi].bitcast(F32),
                                        ALU.subtract).then_inc(w1_lo_ready, 1)

            def split_v_lo(b, n):
                lo, hi = V_PIECES[n]
                dve.wait_ge(v_hi_ready, 2 * (b * len(V_PIECES) + n) + 1)
                nc.vector.tensor_tensor(v_lo[:, b, lo:hi, 0:SH], w2_of(n),
                                        v_hi[:, b, lo:hi, 0:SH].bitcast(F32), ALU.subtract).then_inc(v_lo_ready, 1)
                dve.wait_ge(v_hi_ready, 2 * (b * len(V_PIECES) + n) + 2)
                nc.vector.tensor_tensor(v_lo[:, b, lo:hi, SH:D], we_of(b, n),
                                        v_hi[:, b, lo:hi, SH:D].bitcast(F32), ALU.subtract).then_inc(v_lo_ready, 1)

            def split_l1_lo(b):
                dve.wait_ge(l1_hi_ready, b + 1)
                nc.vector.tensor_tensor(l1_lo[:, b], l1_of(b), l1_hi[:, b].bitcast(F32),
                                        ALU.subtract).then_inc(l1_lo_ready, 1)

            def split_h(s):
                dve.wait_ge(gelu_done, s + 1)
                n = s % H_SLOTS
                nc.vector.tensor_tensor(h_lo[:, n], h_full[:, n], h_hi[:, n].bitcast(F32),
                                        ALU.subtract).then_inc(h_ready, 1)

            def residual_x1(t, c):
                b = t // TPB
                if c < OC - 1:
                    dve.wait_ge(y_done, (OC - 1) * t + c + 1)
                else:
                    dve.wait_ge(b_done, NJ * (t + 1))
                if c == 0 and t % TPB == 0:
                    dve.wait_ge(eb_in[b], 16)
                nc.vector.scalar_tensor_tensor(x1_full[:, t % 2, c], y_ps[c][:], eb_col[:, b, c:c + 1],
                                               x_raw[:, t, c], ALU.add, ALU.add).then_inc(x1_ready, 1)

            def split_x1_lo(t, c):
                if t < NT - 1:
                    dve.wait_ge(x1_hi_ready, OC * t + c + 1)
                else:
                    dve.wait_ge(x1_ready, OC * t + c + 1)
                    if c == 0:
                        dve.wait_ge(z_done, OC * (t - 1))
                    nc.vector.tensor_copy(x1_hi[:, t % 2, c], x1_full[:, t % 2, c]).then_inc(x1_last_hi, 1)
                    dve.wait_ge(x1_last_hi, c + 1)
                nc.vector.tensor_tensor(x1_lo[:, t % 2, c], x1_full[:, t % 2, c],
                                        x1_hi[:, t % 2, c].bitcast(F32), ALU.subtract).then_inc(x1_lo_ready, 1)

            def residual_out(t):
                b = t // TPB
                for n, (c, cols, z) in enumerate(out_parts(t)):
                    dve.wait_ge(z_done, OC * t + n + 1)
                    if t >= 2:
                        dve.wait_ge(stored[t % 2], 16 * OC * (t // 2))
                    nc.vector.scalar_tensor_tensor(o_sb[:, t % 2, c, cols], z[:, cols],
                                                   eb_col[:, b, OC + c:OC + c + 1], x1_full[:, t % 2, c, cols],
                                                   ALU.add, ALU.add).then_inc(o_ready, 1)

            nc.vector.memset(warm[:], 0.0).then_inc(warm_set, 1)
            nc.vector.memset(warm_act[:], 0.0).then_inc(warm_set, 1)
            dve.wait_ge(x_in[0][0], 16)
            nc.vector.tensor_copy(x_hi[:, 0, 0], x_raw[:, 0, 0]).then_inc(x_hi_ready[0][0], 1)
            lo, hi = W1_PIECES[0]
            dve.wait_ge(w1_in[0], 16)
            nc.vector.tensor_copy(w1_hi[:, lo:hi], w1_raw[:, lo:hi]).then_inc(w1_first_ready, 1)
            split_x_lo(0, 0)
            split_w1_lo(0)
            split_x_lo(0, 1)
            split_w1_lo(1)
            split_w1_lo(2)
            split_v_lo(0, 0)
            extra = {0: [(split_w1_lo, 3)], 1: [(split_w1_lo, 4), (split_v_lo, 0, 1)], 2: [(split_v_lo, 0, 2)],
                     4: [(split_l1_lo, 0)]}
            for t in range(1, NT):
                extra[NJ * (t - 1) + 5] = [(split_x_lo, t, k) for k in range(KI)]
            for n in range(len(V_PIECES)):
                extra[NJ * (TPB - 1) + n] = [(split_v_lo, 1, n)]
            extra[NJ * (TPB - 1) + 4] = [(split_l1_lo, 1)]
            for s in range(STEPS):
                if s % NJ == LAG - 1 and s > NJ:
                    for c in range(OC):
                        residual_x1(s // NJ - 1, c)
                split_h(s)
                if s % NJ == LAG - 1 and s > NJ:
                    for c in range(OC):
                        split_x1_lo(s // NJ - 1, c)
                for split, *args in extra.get(s, ()):
                    split(*args)
                if s % NJ == LAG + 3 and s > NJ:
                    residual_out(s // NJ - 1)
            for c in range(OC):
                residual_x1(NT - 1, c)
                split_x1_lo(NT - 1, c)
            residual_out(NT - 1)

        @block.tensor
        def _(pe):
            def product_a(s):
                t, j = divmod(s, NJ)
                if s >= A_BANKS:
                    pe.wait_ge(gelu_done, s - A_BANKS + 1)
                n = piece_of(W1_PIECES, j)
                bank = a_ps[s % A_BANKS]
                for k in range(KI):
                    if j == 0:
                        pe.wait_ge(x_hi_ready[t][k], 1)
                    if s == 0:
                        pe.wait_ge(w1_first_ready, 1)
                    elif t == 0:
                        pe.wait_ge(w1_hi_ready, n)
                    nc.tensor.matmul(bank[:], w1_hi[:, j, k], x_hi[:, t, k], start=(k == 0), stop=False)
                    if j == 0:
                        pe.wait_ge(x_lo_ready, KI * t + k + 1)
                    nc.tensor.matmul(bank[:], w1_hi[:, j, k], x_lo[:, t, k], start=False, stop=False)
                    if t == 0:
                        pe.wait_ge(w1_lo_ready, n + 1)
                    last = nc.tensor.matmul(bank[:], w1_lo[:, j, k], x_hi[:, t, k], start=False, stop=(k == KI - 1))
                last.then_inc(a_done, 1)

            def product_b(s, chunks):
                t, j = divmod(s, NJ)
                b = t // TPB
                pe.wait_ge(h_ready, s + 1)
                if t % TPB == 0:
                    pe.wait_ge(v_lo_ready, 2 * (b * len(V_PIECES) + piece_of(V_PIECES, j)) + 2)
                n = s % H_SLOTS
                for c in chunks:
                    if j == 0 and t >= 1:
                        pe.wait_ge(x1_ready, OC * (t - 1) + c + 1)
                    out_cols = slice(c * P, (c + 1) * P)
                    nc.tensor.matmul(y_ps[c][:], v_lo[:, b, j, out_cols], h_hi[:, n], start=(j == 0), stop=False)
                    nc.tensor.matmul(y_ps[c][:], v_hi[:, b, j, out_cols], h_hi[:, n], start=False, stop=False)
                    last = nc.tensor.matmul(y_ps[c][:], v_hi[:, b, j, out_cols], h_lo[:, n],
                                            start=False, stop=(j == NJ - 1))
                    if c == OC - 1:
                        last.then_inc(b_done, 1)
                    elif j == NJ - 1:
                        last.then_inc(y_done, 1)

            def product_c(t):
                b = t // TPB
                if t % TPB == 0:
                    pe.wait_ge(l1_lo_ready, b + 1)
                for k in range(KI):
                    final = k == KI - 1
                    if t < NT - 1:
                        pe.wait_ge(x1_hi_ready, OC * t + k + 1)
                    else:
                        pe.wait_ge(x1_last_hi, k + 1)
                    for c, cols, bank in out_parts(t):
                        if k == 0 and t >= 1:
                            pe.wait_ge(o_ready, OC * (t - 1) + c + 1)
                        out_cols = slice(c * P, (c + 1) * P)
                        z, hi, lo = bank[:, cols], x1_hi[:, t % 2, k, cols], x1_lo[:, t % 2, k, cols]
                        nc.tensor.matmul(z, l1_lo[:, b, k, out_cols], hi, start=(k == 0), stop=False)
                        nc.tensor.matmul(z, l1_hi[:, b, k, out_cols], hi, start=False, stop=False)
                        pe.wait_ge(x1_lo_ready, OC * t + k + 1)
                        last = nc.tensor.matmul(z, l1_hi[:, b, k, out_cols], lo, start=False, stop=final)
                        if final:
                            last.then_inc(z_done, 1)

            pe.wait_ge(warm_set, 1)
            for _ in range(WARM):
                nc.tensor.matmul(z_ps[0][:, 0:P], warm[:], warm[:], start=True, stop=True)
            for s in range(STEPS):
                product_a(s)
                if s % NJ == LAG + 1 and s > NJ:
                    product_c(s // NJ - 1)
                if s >= LAG:
                    product_b(s - LAG, range(OC))
            for c in range(OC):
                for s in range(STEPS - LAG, STEPS):
                    product_b(s, [c])
            product_c(NT - 1)


def kernel(x, itok_B_0_7, L0_cond_W1, L0_cond_b1, L0_cond_W2, L0_cond_b2, L0_cond_We, L0_cond_be,
           L1_cond_weight, L1_cond_bias):
    import numpy as np
    import concourse.bacc as bacc
    from concourse.bass_utils import run_bass_kernel_spmd

    x, idx, W1, b1, W2, b2, We, be, L1, l1b = (np.asarray(a) for a in (
        x, itok_B_0_7, L0_cond_W1, L0_cond_b1, L0_cond_W2, L0_cond_b2, L0_cond_We, L0_cond_be,
        L1_cond_weight, L1_cond_bias))
    B, N, D = x.shape
    HID = W1.shape[1]
    E, _, PART = We.shape
    KI, NJ, NT = D // P, HID // P, B * N // TOK

    xT = x.reshape(NT, TOK, KI, P).transpose(0, 3, 2, 1)
    w1 = W1.reshape(KI, P, NJ, P).transpose(1, 2, 0, 3)
    b1c = b1.reshape(NJ, P).T
    w2 = W2.reshape(NJ, P, D - PART).transpose(1, 0, 2)
    we = We.reshape(E, NJ, P, PART).transpose(0, 2, 1, 3).reshape(E, P, NJ * PART)
    l1 = L1.transpose(0, 2, 1).reshape(E, KI, P, D).transpose(0, 2, 1, 3).reshape(E, P, KI * D)
    expert_w = np.concatenate([we, l1], axis=2)
    yb = np.concatenate([np.broadcast_to(b2, (E, D - PART)), be], axis=1).reshape(E, KI, P).transpose(0, 2, 1)
    zb = l1b.reshape(E, KI, P).transpose(0, 2, 1)
    expert_b = np.concatenate([yb, zb], axis=2)

    nc = bacc.Bacc("TRN2", target_bir_lowering=False, num_devices=1)
    arrays, aps = {}, []
    for name, a in [("xT", xT), ("idx", idx.reshape(1, B)), ("w1", w1), ("b1", b1c), ("w2", w2),
                    ("expert_w", expert_w), ("expert_b", expert_b)]:
        a = np.ascontiguousarray(a)
        arrays[name] = a
        aps.append(nc.dram_tensor(name, a.shape, mybir.dt.from_np(a.dtype), kind="ExternalInput").ap())
    out = nc.dram_tensor("out", (NT, P, KI, TOK), F32, kind="ExternalOutput").ap()
    two_layer_kernel(nc, *aps, out)
    r = run_bass_kernel_spmd(nc, [arrays], core_ids=[0])
    got = np.asarray(r.results[0]["out"])
    return np.ascontiguousarray(got.transpose(0, 3, 2, 1)).reshape(B, N, D)
```

```python
from contextlib import ExitStack

import concourse.bass as bass
from concourse import mybir

F32 = mybir.dt.float32
F32R = mybir.dt.float32r
I32 = mybir.dt.int32
ACT = mybir.ActivationFunctionType
ALU = mybir.AluOpType

P = 128
TOK = 512
A_BANKS = 4
H_SLOTS = 5
LAG = 3
WARM = 28


def two_layer_kernel(nc, xT, idx, w1, b1, w2, expert_w, expert_b, out):
    NT, _, KI, _ = xT.shape
    _, NJ, _, _ = w1.shape
    B = idx.shape[1]
    E = expert_w.shape[0]
    SH = w2.shape[2]
    D = KI * P
    PART = D - SH
    OC = D // P
    TPB = NT // B
    STEPS = NT * NJ
    W1_PIECES = [(0, 1), (1, 2), (2, 4), (4, 6), (6, NJ)]
    V_PIECES = [(0, 2), (2, 4), (4, NJ)]

    def piece_of(pieces, j):
        return next(n for n, (lo, hi) in enumerate(pieces) if lo <= j < hi)

    with ExitStack() as ctx:
        def sb(name, shape, dt=F32):
            return ctx.enter_context(nc.sbuf_tensor(name, shape, dt))

        def sem(name):
            return ctx.enter_context(nc.semaphore(name))

        x_raw = sb("x_raw", [P, NT, KI, TOK])
        x_hi = sb("x_hi", [P, NT, KI, TOK], F32R)
        x_lo = sb("x_lo", [P, NT, KI, TOK], F32R)
        w1_raw = sb("w1_raw", [P, NJ, KI, P])
        w1_hi = sb("w1_hi", [P, NJ, KI, P], F32R)
        w1_lo = sb("w1_lo", [P, NJ, KI, P], F32R)
        w2_raw = sb("w2_raw", [P, NJ, SH])
        ex_raw = sb("ex_raw", [P, B, NJ * PART + KI * D])
        v_hi = sb("v_hi", [P, B, NJ, D], F32R)
        v_lo = sb("v_lo", [P, B, NJ, D], F32R)
        l1_hi = sb("l1_hi", [P, B, KI, D], F32R)
        l1_lo = sb("l1_lo", [P, B, KI, D], F32R)
        b1_col = sb("b1_col", [P, NJ])
        eb_col = sb("eb_col", [P, B, 2 * KI])
        idx_sb = sb("idx_sb", [1, B], I32)
        h_full = sb("h_full", [P, H_SLOTS, TOK])
        h_hi = sb("h_hi", [P, H_SLOTS, TOK], F32R)
        h_lo = sb("h_lo", [P, H_SLOTS, TOK], F32R)
        x1_full = sb("x1_full", [P, 2, OC, TOK])
        x1_hi = sb("x1_hi", [P, 2, OC, TOK], F32R)
        x1_lo = sb("x1_lo", [P, 2, OC, TOK], F32R)
        o_sb = sb("o_sb", [P, 2, OC, TOK])
        warm = sb("warm", [P, P], mybir.dt.bfloat16)
        warm_act = sb("warm_act", [P, 1])

        a_ps = [ctx.enter_context(nc.psum_tensor(f"a_ps{n}", [P, TOK], F32)) for n in range(A_BANKS)]
        y_ps = [ctx.enter_context(nc.psum_tensor(f"y_ps{n}", [P, TOK], F32)) for n in range(OC)]
        z_ps = [ctx.enter_context(nc.psum_tensor(f"z_ps{n}", [P, TOK], F32)) for n in range(OC)]

        def columns(t):
            return [slice(0, TOK)] if t < NT - 1 else [slice(0, TOK // 2), slice(TOK // 2, TOK)]

        def z_bank(c, n):
            return z_ps[c] if n == 0 else a_ps[c]

        def x1_count(t, c, n):
            return OC * t + c * len(columns(t)) + n + 1

        def out_count(t, c, n):
            return OC * t + n * OC + c + 1

        idx_in = sem("idx_in")
        b1_in = sem("b1_in")
        w1_in = [sem(f"w1_in{n}") for n in range(len(W1_PIECES))]
        x_in = [[sem(f"x_in{t}_{k}") for k in range(KI)] for t in range(NT)]
        w2_in = [sem(f"w2_in{n}") for n in range(len(V_PIECES))]
        ex_in = [sem(f"ex_in{b}") for b in range(B)]
        eb_in = [sem(f"eb_in{b}") for b in range(B)]
        warm_set = sem("warm_set")
        x_hi_ready = [[sem(f"x_hi_ready{t}_{k}") for k in range(KI)] for t in range(NT)]
        x_lo_ready = sem("x_lo_ready")
        w1_hi_ready = sem("w1_hi_ready")
        w1_first_ready = sem("w1_first_ready")
        w1_lo_ready = sem("w1_lo_ready")
        v_hi_ready = sem("v_hi_ready")
        v_lo_ready = sem("v_lo_ready")
        l1_hi_ready = sem("l1_hi_ready")
        l1_lo_ready = sem("l1_lo_ready")
        a_done = sem("a_done")
        gelu_done = sem("gelu_done")
        h_ready = sem("h_ready")
        b_done = sem("b_done")
        y_done = sem("y_done")
        x1_ready = sem("x1_ready")
        x1_hi_ready = sem("x1_hi_ready")
        x1_lo_ready = sem("x1_lo_ready")
        z_done = sem("z_done")
        o_ready = sem("o_ready")
        stored = [sem(f"stored{n}") for n in range(2)]

        block = ctx.enter_context(nc.Block())

        @block.sync
        def _(sp):
            def load_w1(n):
                lo, hi = W1_PIECES[n]
                sp.dma_start(w1_raw[:, lo:hi], w1[:, lo:hi]).then_inc(w1_in[n], 16)

            def load_w2(n):
                lo, hi = V_PIECES[n]
                sp.dma_start(w2_raw[:, lo:hi], w2[:, lo:hi]).then_inc(w2_in[n], 16)

            def load_x(t, k):
                sp.dma_start(x_raw[:, t, k], xT[t, :, k]).then_inc(x_in[t][k], 16)

            load_x(0, 0)
            load_w1(0)
            load_x(0, 1)
            load_w1(1)
            load_w1(2)
            load_w2(0)
            sp.wait_ge(idx_in, 16)
            expert = [sp.value_load(idx_sb[0:1, b:b + 1], min_val=0, max_val=E - 1) for b in range(B)]

            def load_expert(b):
                sp.dma_start(ex_raw[:, b], expert_w[bass.ds(expert[b], 1)].rearrange("e p n -> p (e n)"))\
                    .then_inc(ex_in[b], 16)
                sp.dma_start(eb_col[:, b], expert_b[bass.ds(expert[b], 1)].rearrange("e p n -> p (e n)"))\
                    .then_inc(eb_in[b], 16)

            load_expert(0)
            load_w1(3)
            load_w2(1)
            load_w1(4)
            load_w2(2)
            for t in range(1, NT):
                for k in range(KI):
                    load_x(t, k)
                if t < B:
                    load_expert(t)
            for t in range(NT):
                for n, cols in enumerate(columns(t)):
                    for c in range(OC):
                        sp.wait_ge(o_ready, out_count(t, c, n))
                        sp.dma_start(out[t, :, c, cols], o_sb[:, t % 2, c, cols]).then_inc(stored[t % 2], 16)
            for n in range(2):
                sp.wait_ge(stored[n], 16 * OC * sum(len(columns(t)) for t in range(n, NT, 2)))

        def w2_of(n):
            lo, hi = V_PIECES[n]
            return w2_raw[:, lo:hi]

        def we_of(b, n):
            lo, hi = V_PIECES[n]
            return ex_raw[:, b, 0:NJ * PART].rearrange("p (j c) -> p j c", j=NJ)[:, lo:hi]

        def l1_of(b):
            return ex_raw[:, b, NJ * PART:].rearrange("p (k c) -> p k c", k=KI)

        @block.gpsimd
        def _(pool):
            pool.dma_start(idx_sb[:], idx).then_inc(idx_in, 16)
            pool.dma_start(b1_col[:], b1).then_inc(b1_in, 16)

        @block.scalar
        def _(act):
            def split_x_hi(t, k):
                act.wait_ge(x_in[t][k], 16)
                nc.scalar.activation(x_hi[:, t, k], x_raw[:, t, k], ACT.Copy).then_inc(x_hi_ready[t][k], 1)

            def split_w1_hi(n):
                lo, hi = W1_PIECES[n]
                act.wait_ge(w1_in[n], 16)
                nc.scalar.activation(w1_hi[:, lo:hi], w1_raw[:, lo:hi], ACT.Copy).then_inc(w1_hi_ready, 1)

            def split_v_hi(b, n):
                lo, hi = V_PIECES[n]
                act.wait_ge(w2_in[n], 16)
                nc.scalar.activation(v_hi[:, b, lo:hi, 0:SH], w2_of(n), ACT.Copy).then_inc(v_hi_ready, 1)
                act.wait_ge(ex_in[b], 16)
                nc.scalar.activation(v_hi[:, b, lo:hi, SH:D], we_of(b, n), ACT.Copy).then_inc(v_hi_ready, 1)

            def split_l1_hi(b):
                act.wait_ge(ex_in[b], 16)
                nc.scalar.activation(l1_hi[:, b], l1_of(b), ACT.Copy).then_inc(l1_hi_ready, 1)

            def gelu(s):
                act.wait_ge(a_done, s + 1)
                if s >= H_SLOTS:
                    act.wait_ge(b_done, s - H_SLOTS + 1)
                j = s % NJ
                nc.scalar.activation(h_hi[:, s % H_SLOTS], a_ps[s % A_BANKS][:], ACT.Gelu, bias=b1_col[:, j:j + 1])
                nc.scalar.activation(h_full[:, s % H_SLOTS], a_ps[s % A_BANKS][:], ACT.Gelu,
                                     bias=b1_col[:, j:j + 1]).then_inc(gelu_done, 1)

            def split_x1_hi(t, c):
                for n, cols in enumerate(columns(t)):
                    act.wait_ge(x1_ready, x1_count(t, c, n))
                    if t >= 2:
                        act.wait_ge(z_done, OC * (t - 1))
                    nc.scalar.activation(x1_hi[:, t % 2, c, cols], x1_full[:, t % 2, c, cols],
                                         ACT.Copy).then_inc(x1_hi_ready, 1)

            act.wait_ge(warm_set, 2)
            nc.scalar.activation(warm_act[:], warm_act[:], ACT.Gelu)
            split_x_hi(0, 1)
            split_w1_hi(1)
            split_w1_hi(2)
            split_v_hi(0, 0)
            act.wait_ge(b1_in, 16)

            def split_ahead(s):
                t, j = divmod(s, NJ)
                if s == 0:
                    split_w1_hi(3)
                if s == 1:
                    split_w1_hi(4)
                    split_v_hi(0, 1)
                if s == 2:
                    split_v_hi(0, 2)
                if s == 4:
                    split_l1_hi(0)
                if j == 5 and t < NT - 1:
                    for k in range(KI):
                        split_x_hi(t + 1, k)
                if t == TPB - 1 and j < len(V_PIECES):
                    split_v_hi(1, j)
                if t == TPB - 1 and j == 4:
                    split_l1_hi(1)

            for s in range(STEPS):
                if s % NJ == LAG and s > NJ:
                    for c in range(OC):
                        split_x1_hi(s // NJ - 1, c)
                gelu(s)
                split_ahead(s)
            for c in range(OC):
                split_x1_hi(NT - 1, c)

        @block.vector
        def _(dve):
            def split_x_lo(t, k):
                dve.wait_ge(x_hi_ready[t][k], 1)
                nc.vector.tensor_tensor(x_lo[:, t, k], x_raw[:, t, k], x_hi[:, t, k].bitcast(F32),
                                        ALU.subtract).then_inc(x_lo_ready, 1)

            def split_w1_lo(n):
                lo, hi = W1_PIECES[n]
                if n == 0:
                    dve.wait_ge(w1_first_ready, 1)
                else:
                    dve.wait_ge(w1_hi_ready, n)
                nc.vector.tensor_tensor(w1_lo[:, lo:hi], w1_raw[:, lo:hi], w1_hi[:, lo:hi].bitcast(F32),
                                        ALU.subtract).then_inc(w1_lo_ready, 1)

            def split_v_lo(b, n):
                lo, hi = V_PIECES[n]
                dve.wait_ge(v_hi_ready, 2 * (b * len(V_PIECES) + n) + 1)
                nc.vector.tensor_tensor(v_lo[:, b, lo:hi, 0:SH], w2_of(n),
                                        v_hi[:, b, lo:hi, 0:SH].bitcast(F32), ALU.subtract).then_inc(v_lo_ready, 1)
                dve.wait_ge(v_hi_ready, 2 * (b * len(V_PIECES) + n) + 2)
                nc.vector.tensor_tensor(v_lo[:, b, lo:hi, SH:D], we_of(b, n),
                                        v_hi[:, b, lo:hi, SH:D].bitcast(F32), ALU.subtract).then_inc(v_lo_ready, 1)

            def split_l1_lo(b):
                dve.wait_ge(l1_hi_ready, b + 1)
                nc.vector.tensor_tensor(l1_lo[:, b], l1_of(b), l1_hi[:, b].bitcast(F32),
                                        ALU.subtract).then_inc(l1_lo_ready, 1)

            def split_h(s):
                dve.wait_ge(gelu_done, s + 1)
                n = s % H_SLOTS
                nc.vector.tensor_tensor(h_lo[:, n], h_full[:, n], h_hi[:, n].bitcast(F32),
                                        ALU.subtract).then_inc(h_ready, 1)

            def residual_x1(t, c):
                b = t // TPB
                if c < OC - 1:
                    dve.wait_ge(y_done, (OC - 1) * t + c + 1)
                else:
                    dve.wait_ge(b_done, NJ * (t + 1))
                if c == 0 and t % TPB == 0:
                    dve.wait_ge(eb_in[b], 16)
                for cols in columns(t):
                    nc.vector.scalar_tensor_tensor(x1_full[:, t % 2, c, cols], y_ps[c][:, cols], eb_col[:, b, c:c + 1],
                                                   x_raw[:, t, c, cols], ALU.add, ALU.add).then_inc(x1_ready, 1)

            def split_x1_lo(t, c):
                for n, cols in enumerate(columns(t)):
                    dve.wait_ge(x1_hi_ready, x1_count(t, c, n))
                    nc.vector.tensor_tensor(x1_lo[:, t % 2, c, cols], x1_full[:, t % 2, c, cols],
                                            x1_hi[:, t % 2, c, cols].bitcast(F32),
                                            ALU.subtract).then_inc(x1_lo_ready, 1)

            def residual_out(t):
                b = t // TPB
                if t >= 2:
                    dve.wait_ge(stored[t % 2], 16 * OC * (t // 2))
                for n, cols in enumerate(columns(t)):
                    for c in range(OC):
                        dve.wait_ge(z_done, out_count(t, c, n))
                        nc.vector.scalar_tensor_tensor(o_sb[:, t % 2, c, cols], z_bank(c, n)[:, cols],
                                                       eb_col[:, b, OC + c:OC + c + 1], x1_full[:, t % 2, c, cols],
                                                       ALU.add, ALU.add).then_inc(o_ready, 1)

            nc.vector.memset(warm[:], 0.0).then_inc(warm_set, 1)
            nc.vector.memset(warm_act[:], 0.0).then_inc(warm_set, 1)
            dve.wait_ge(x_in[0][0], 16)
            nc.vector.tensor_copy(x_hi[:, 0, 0], x_raw[:, 0, 0]).then_inc(x_hi_ready[0][0], 1)
            lo, hi = W1_PIECES[0]
            dve.wait_ge(w1_in[0], 16)
            nc.vector.tensor_copy(w1_hi[:, lo:hi], w1_raw[:, lo:hi]).then_inc(w1_first_ready, 1)
            split_x_lo(0, 0)
            split_w1_lo(0)
            split_x_lo(0, 1)
            split_w1_lo(1)
            split_w1_lo(2)
            split_v_lo(0, 0)

            def split_ahead(s):
                t, j = divmod(s, NJ)
                if s == 0:
                    split_w1_lo(3)
                if s == 1:
                    split_w1_lo(4)
                    split_v_lo(0, 1)
                if s == 2:
                    split_v_lo(0, 2)
                if s == 4:
                    split_l1_lo(0)
                if j == 5 and t < NT - 1:
                    for k in range(KI):
                        split_x_lo(t + 1, k)
                if t == TPB - 1 and j < len(V_PIECES):
                    split_v_lo(1, j)
                if t == TPB - 1 and j == 4:
                    split_l1_lo(1)

            for s in range(STEPS):
                if s % NJ == LAG - 1 and s > NJ:
                    for c in range(OC):
                        residual_x1(s // NJ - 1, c)
                split_h(s)
                if s % NJ == LAG - 1 and s > NJ:
                    for c in range(OC):
                        split_x1_lo(s // NJ - 1, c)
                split_ahead(s)
                if s % NJ == LAG + 3 and s > NJ:
                    residual_out(s // NJ - 1)
            for c in range(OC):
                residual_x1(NT - 1, c)
                split_x1_lo(NT - 1, c)
            residual_out(NT - 1)

        @block.tensor
        def _(pe):
            def product_a(s):
                t, j = divmod(s, NJ)
                if s >= A_BANKS:
                    pe.wait_ge(gelu_done, s - A_BANKS + 1)
                n = piece_of(W1_PIECES, j)
                bank = a_ps[s % A_BANKS]
                for k in range(KI):
                    if j == 0:
                        pe.wait_ge(x_hi_ready[t][k], 1)
                    if s == 0:
                        pe.wait_ge(w1_first_ready, 1)
                    elif t == 0:
                        pe.wait_ge(w1_hi_ready, n)
                    nc.tensor.matmul(bank[:], w1_hi[:, j, k], x_hi[:, t, k], start=(k == 0), stop=False)
                    if j == 0:
                        pe.wait_ge(x_lo_ready, KI * t + k + 1)
                    nc.tensor.matmul(bank[:], w1_hi[:, j, k], x_lo[:, t, k], start=False, stop=False)
                    if t == 0:
                        pe.wait_ge(w1_lo_ready, n + 1)
                    last = nc.tensor.matmul(bank[:], w1_lo[:, j, k], x_hi[:, t, k], start=False, stop=(k == KI - 1))
                last.then_inc(a_done, 1)

            def product_b(s, chunks):
                t, j = divmod(s, NJ)
                b = t // TPB
                pe.wait_ge(h_ready, s + 1)
                if t % TPB == 0:
                    pe.wait_ge(v_lo_ready, 2 * (b * len(V_PIECES) + piece_of(V_PIECES, j)) + 2)
                n = s % H_SLOTS
                for c in chunks:
                    if j == 0 and t >= 1:
                        pe.wait_ge(x1_ready, OC * (t - 1) + c + 1)
                    out_cols = slice(c * P, (c + 1) * P)
                    nc.tensor.matmul(y_ps[c][:], v_lo[:, b, j, out_cols], h_hi[:, n], start=(j == 0), stop=False)
                    nc.tensor.matmul(y_ps[c][:], v_hi[:, b, j, out_cols], h_hi[:, n], start=False, stop=False)
                    last = nc.tensor.matmul(y_ps[c][:], v_hi[:, b, j, out_cols], h_lo[:, n],
                                            start=False, stop=(j == NJ - 1))
                    if c == OC - 1:
                        last.then_inc(b_done, 1)
                    elif j == NJ - 1:
                        last.then_inc(y_done, 1)

            def product_c(t):
                b = t // TPB
                if t % TPB == 0:
                    pe.wait_ge(l1_lo_ready, b + 1)
                for k in range(KI):
                    for n, cols in enumerate(columns(t)):
                        hi, lo = x1_hi[:, t % 2, k, cols], x1_lo[:, t % 2, k, cols]
                        pe.wait_ge(x1_hi_ready, x1_count(t, k, n))
                        for c in range(OC):
                            if k == 0 and n == 0 and t >= 1:
                                pe.wait_ge(o_ready, OC * (t - 1) + c + 1)
                            z, out_cols = z_bank(c, n)[:, cols], slice(c * P, (c + 1) * P)
                            nc.tensor.matmul(z, l1_lo[:, b, k, out_cols], hi, start=(k == 0), stop=False)
                            nc.tensor.matmul(z, l1_hi[:, b, k, out_cols], hi, start=False, stop=False)
                        pe.wait_ge(x1_lo_ready, x1_count(t, k, n))
                        for c in range(OC):
                            z, out_cols = z_bank(c, n)[:, cols], slice(c * P, (c + 1) * P)
                            last = nc.tensor.matmul(z, l1_hi[:, b, k, out_cols], lo, start=False, stop=(k == KI - 1))
                            if k == KI - 1:
                                last.then_inc(z_done, 1)

            pe.wait_ge(warm_set, 1)
            for _ in range(WARM):
                nc.tensor.matmul(z_ps[0][:, 0:P], warm[:], warm[:], start=True, stop=True)
            for s in range(STEPS):
                product_a(s)
                if s % NJ == LAG + 1 and s > NJ:
                    product_c(s // NJ - 1)
                if s >= LAG:
                    product_b(s - LAG, range(OC))
            for c in range(OC):
                for s in range(STEPS - LAG, STEPS):
                    product_b(s, [c])
            product_c(NT - 1)


def kernel(x, itok_B_0_7, L0_cond_W1, L0_cond_b1, L0_cond_W2, L0_cond_b2, L0_cond_We, L0_cond_be,
           L1_cond_weight, L1_cond_bias):
    import numpy as np
    import concourse.bacc as bacc
    from concourse.bass_utils import run_bass_kernel_spmd

    x, idx, W1, b1, W2, b2, We, be, L1, l1b = (np.asarray(a) for a in (
        x, itok_B_0_7, L0_cond_W1, L0_cond_b1, L0_cond_W2, L0_cond_b2, L0_cond_We, L0_cond_be,
        L1_cond_weight, L1_cond_bias))
    B, N, D = x.shape
    HID = W1.shape[1]
    E, _, PART = We.shape
    KI, NJ, NT = D // P, HID // P, B * N // TOK

    xT = x.reshape(NT, TOK, KI, P).transpose(0, 3, 2, 1)
    w1 = W1.reshape(KI, P, NJ, P).transpose(1, 2, 0, 3)
    b1c = b1.reshape(NJ, P).T
    w2 = W2.reshape(NJ, P, D - PART).transpose(1, 0, 2)
    we = We.reshape(E, NJ, P, PART).transpose(0, 2, 1, 3).reshape(E, P, NJ * PART)
    l1 = L1.transpose(0, 2, 1).reshape(E, KI, P, D).transpose(0, 2, 1, 3).reshape(E, P, KI * D)
    expert_w = np.concatenate([we, l1], axis=2)
    yb = np.concatenate([np.broadcast_to(b2, (E, D - PART)), be], axis=1).reshape(E, KI, P).transpose(0, 2, 1)
    zb = l1b.reshape(E, KI, P).transpose(0, 2, 1)
    expert_b = np.concatenate([yb, zb], axis=2)

    nc = bacc.Bacc("TRN2", target_bir_lowering=False, num_devices=1)
    arrays, aps = {}, []
    for name, a in [("xT", xT), ("idx", idx.reshape(1, B)), ("w1", w1), ("b1", b1c), ("w2", w2),
                    ("expert_w", expert_w), ("expert_b", expert_b)]:
        a = np.ascontiguousarray(a)
        arrays[name] = a
        aps.append(nc.dram_tensor(name, a.shape, mybir.dt.from_np(a.dtype), kind="ExternalInput").ap())
    out = nc.dram_tensor("out", (NT, P, KI, TOK), F32, kind="ExternalOutput").ap()
    two_layer_kernel(nc, *aps, out)
    r = run_bass_kernel_spmd(nc, [arrays], core_ids=[0])
    got = np.asarray(r.results[0]["out"])
    return np.ascontiguousarray(got.transpose(0, 3, 2, 1)).reshape(B, N, D)
```
